# Optimizing a Trainium2 kernel written in Bass

```python
import numpy as np
import jax
import jax.numpy as jnp

def _softmax(x, axis=-1):
    return jax.nn.softmax(x, axis=axis)

def _gelu(x):
    return jax.nn.gelu(x, approximate=True)

def _silu(x):
    return jax.nn.silu(x)

def _sigmoid(x):
    return jax.nn.sigmoid(x)

def _layernorm(x, axis=-1, eps=1e-05):
    m = jnp.mean(x, axis=axis, keepdims=True)
    v = jnp.var(x, axis=axis, keepdims=True)
    return (x - m) / jnp.sqrt(v + eps)

def _scatter_add(tgt, idx, src, axis=0):
    return tgt.at[idx].add(src)

def _segment_sum(src, seg, n):
    return jax.ops.segment_sum(src, seg, n)
kernel_name = 'mk_macaron_d1_jaxref_r4_317058'

def setup_inputs(seed: int=0):
    np.random.seed(seed)
    _w = jnp.asarray

    def _L0_attn_setup():
        import jax, jax.numpy as jnp
        import numpy as np
        D_MODEL, D_STATE, D_CONV, EXPAND, DT_RANK = (256, 16, 4, 2, 32)
        D_INNER = D_MODEL * EXPAND

        def _ssm_forward(x, Wi, bi, conv_w, conv_b, Wdt, bdt, A_log, Bm, Cm, Dv, Wo, bo):
            Bb, T, _ = x.shape
            xz = x @ Wi.T + bi
            x_in, z = (xz[..., :D_INNER], xz[..., D_INNER:])
            xc = jnp.transpose(x_in, (0, 2, 1))
            xc = jax.lax.conv_general_dilated(xc, conv_w, (1,), [(D_CONV - 1, 0)], dimension_numbers=('NCH', 'OIH', 'NCH'), feature_group_count=D_INNER)
            xc = xc + conv_b[None, :, None]
            u = jax.nn.silu(jnp.transpose(xc, (0, 2, 1)))
            dt = jax.nn.softplus(x_in[..., :DT_RANK] @ Wdt.T + bdt)
            A = -jnp.exp(A_log)

            def step(h, inp):
                dt_t, u_t = inp
                h = h * jnp.exp(dt_t[:, :, None] * A[None]) + dt_t[:, :, None] * Bm[None] * u_t[:, :, None]
                y = jnp.einsum('bdn,dn->bd', h, Cm)
                return (h, y)
            h0 = jnp.zeros((Bb, D_INNER, D_STATE), x.dtype)
            _, ys = jax.lax.scan(step, h0, (jnp.swapaxes(dt, 0, 1), jnp.swapaxes(u, 0, 1)))
            out = jnp.swapaxes(ys, 0, 1) * jax.nn.silu(z)
            return out @ Wo.T + bo + x * Dv.mean()
        key = jax.random.key(seed)
        ks = jax.random.split(key, 12)
        B, T = (4, 512)
        s_in = 1.0 / np.sqrt(D_MODEL)
        s_dt = 1.0 / np.sqrt(DT_RANK)
        s_out = 1.0 / np.sqrt(D_INNER)
        return {'x': jax.random.normal(ks[0], (B, T, D_MODEL), jnp.float32), 'Wi': jax.random.uniform(ks[1], (2 * D_INNER, D_MODEL), jnp.float32, -s_in, s_in), 'bi': jax.random.uniform(ks[2], (2 * D_INNER,), jnp.float32, -s_in, s_in), 'conv_w': jax.random.uniform(ks[3], (D_INNER, 1, D_CONV), jnp.float32, -0.5, 0.5), 'conv_b': jax.random.uniform(ks[4], (D_INNER,), jnp.float32, -0.5, 0.5), 'Wdt': jax.random.uniform(ks[5], (D_INNER, DT_RANK), jnp.float32, -s_dt, s_dt), 'bdt': jax.random.uniform(ks[6], (D_INNER,), jnp.float32, -s_dt, s_dt), 'A_log': jnp.log(0.99 - jax.random.uniform(ks[7], (D_INNER, D_STATE), jnp.float32) * 0.01), 'Bm': jax.random.normal(ks[8], (D_INNER, D_STATE), jnp.float32) * 0.01, 'Cm': jax.random.normal(ks[9], (D_INNER, D_STATE), jnp.float32) * 0.01, 'Dv': jnp.ones((D_INNER,), jnp.float32) * 0.1, 'Wo': jax.random.uniform(ks[10], (D_MODEL, D_INNER), jnp.float32, -s_out, s_out), 'bo': jax.random.uniform(ks[11], (D_MODEL,), jnp.float32, -s_out, s_out)}
    _L0_attn_in = _L0_attn_setup()

    def _L0_ffn_setup():
        import jax, jax.numpy as jnp
        import numpy as np
        NUM_GEMMS = 8
        HIDDEN = 256
        INTER = 1024
        key = jax.random.key(seed)
        k_x, k_w1, k_b1, k_w2, k_b2 = jax.random.split(key, 5)
        x = jax.random.normal(k_x, (8, 512, HIDDEN), dtype=jnp.float32)
        s1 = 1.0 / np.sqrt(HIDDEN)
        s2 = 1.0 / np.sqrt(INTER)
        W1 = jax.random.uniform(k_w1, (NUM_GEMMS, INTER, HIDDEN), jnp.float32, -s1, s1)
        b1 = jax.random.uniform(k_b1, (NUM_GEMMS, INTER), jnp.float32, -s1, s1)
        W2 = jax.random.uniform(k_w2, (NUM_GEMMS, HIDDEN, INTER), jnp.float32, -s2, s2)
        b2 = jax.random.uniform(k_b2, (NUM_GEMMS, HIDDEN), jnp.float32, -s2, s2)
        return {'x': x, 'W1': W1, 'b1': b1, 'W2': W2, 'b2': b2}
    _L0_ffn_in = _L0_ffn_setup()
    _d = {'L0_attn_x': _L0_attn_in['x'], 'L0_attn_Wi': _L0_attn_in['Wi'], 'L0_attn_bi': _L0_attn_in['bi'], 'L0_attn_conv_w': _L0_attn_in['conv_w'], 'L0_attn_conv_b': _L0_attn_in['conv_b'], 'L0_attn_Wdt': _L0_attn_in['Wdt'], 'L0_attn_bdt': _L0_attn_in['bdt'], 'L0_attn_A_log': _L0_attn_in['A_log'], 'L0_attn_Bm': _L0_attn_in['Bm'], 'L0_attn_Cm': _L0_attn_in['Cm'], 'L0_attn_Dv': _L0_attn_in['Dv'], 'L0_attn_Wo': _L0_attn_in['Wo'], 'L0_attn_bo': _L0_attn_in['bo'], 'L0_ffn_W1': _L0_ffn_in['W1'], 'L0_ffn_b1': _L0_ffn_in['b1'], 'L0_ffn_W2': _L0_ffn_in['W2'], 'L0_ffn_b2': _L0_ffn_in['b2']}
    _x0 = _d['L0_attn_x']
    _d['L0_attn_x'] = jax.random.normal(jax.random.fold_in(jax.random.key(seed), 1), (2, 2048, 256), dtype=_x0.dtype)
    del _x0
    return _d

def reference(L0_attn_x, L0_attn_Wi, L0_attn_bi, L0_attn_conv_w, L0_attn_conv_b, L0_attn_Wdt, L0_attn_bdt, L0_attn_A_log, L0_attn_Bm, L0_attn_Cm, L0_attn_Dv, L0_attn_Wo, L0_attn_bo, L0_ffn_W1, L0_ffn_b1, L0_ffn_W2, L0_ffn_b2):

    def _L0_attn_ref(x, Wi, bi, conv_w, conv_b, Wdt, bdt, A_log, Bm, Cm, Dv, Wo, bo):
        import jax, jax.numpy as jnp
        import numpy as np
        D_MODEL, D_STATE, D_CONV, EXPAND, DT_RANK = (256, 16, 4, 2, 32)
        D_INNER = D_MODEL * EXPAND

        def _ssm_forward(x, Wi, bi, conv_w, conv_b, Wdt, bdt, A_log, Bm, Cm, Dv, Wo, bo):
            Bb, T, _ = x.shape
            xz = x @ Wi.T + bi
            x_in, z = (xz[..., :D_INNER], xz[..., D_INNER:])
            xc = jnp.transpose(x_in, (0, 2, 1))
            xc = jax.lax.conv_general_dilated(xc, conv_w, (1,), [(D_CONV - 1, 0)], dimension_numbers=('NCH', 'OIH', 'NCH'), feature_group_count=D_INNER)
            xc = xc + conv_b[None, :, None]
            u = jax.nn.silu(jnp.transpose(xc, (0, 2, 1)))
            dt = jax.nn.softplus(x_in[..., :DT_RANK] @ Wdt.T + bdt)
            A = -jnp.exp(A_log)

            def step(h, inp):
                dt_t, u_t = inp
                h = h * jnp.exp(dt_t[:, :, None] * A[None]) + dt_t[:, :, None] * Bm[None] * u_t[:, :, None]
                y = jnp.einsum('bdn,dn->bd', h, Cm)
                return (h, y)
            h0 = jnp.zeros((Bb, D_INNER, D_STATE), x.dtype)
            _, ys = jax.lax.scan(step, h0, (jnp.swapaxes(dt, 0, 1), jnp.swapaxes(u, 0, 1)))
            out = jnp.swapaxes(ys, 0, 1) * jax.nn.silu(z)
            return out @ Wo.T + bo + x * Dv.mean()
        return _ssm_forward(x, Wi, bi, conv_w, conv_b, Wdt, bdt, A_log, Bm, Cm, Dv, Wo, bo)

    def _L0_ffn_ref(x, W1, b1, W2, b2):
        import jax, jax.numpy as jnp
        import numpy as np
        NUM_GEMMS = 8
        HIDDEN = 256
        INTER = 1024
        orig_shape = x.shape
        token_num = int(np.prod(orig_shape[:-1]))
        m = token_num // NUM_GEMMS
        xg = x.reshape(NUM_GEMMS, m, HIDDEN)
        h1 = jnp.einsum('gmh,goh->gmo', xg, W1) + b1[:, None, :]
        h2 = jnp.einsum('gmo,gho->gmh', h1, W2) + b2[:, None, :]
        return h2.reshape(orig_shape)
    x = L0_attn_x
    x = x + 0.5 * _L0_ffn_ref(_layernorm(x, axis=-1), L0_ffn_W1, L0_ffn_b1, L0_ffn_W2, L0_ffn_b2)
    x = x + _L0_attn_ref(_layernorm(x, axis=-1), L0_attn_Wi, L0_attn_bi, L0_attn_conv_w, L0_attn_conv_b, L0_attn_Wdt, L0_attn_bdt, L0_attn_A_log, L0_attn_Bm, L0_attn_Cm, L0_attn_Dv, L0_attn_Wo, L0_attn_bo)
    x = x + 0.5 * _L0_ffn_ref(_layernorm(x, axis=-1), L0_ffn_W1, L0_ffn_b1, L0_ffn_W2, L0_ffn_b2)
    return x

_drawn_inputs = setup_inputs


def setup_inputs(seed=0):
    import zlib

    import numpy as np

    out = dict(_drawn_inputs(seed))
    spreads = {'L0_attn_Dv': (0.10000000149011612, 0.6)}
    factors = {'L0_attn_Wi': 8.0,
     'L0_attn_bi': 8.0,
     'L0_attn_conv_w': 8.0,
     'L0_attn_conv_b': 8.0,
     'L0_attn_Wdt': 8.0,
     'L0_attn_bdt': 8.0,
     'L0_attn_A_log': 64.0,
     'L0_attn_Bm': 8.0,
     'L0_attn_Cm': 8.0,
     'L0_attn_Wo': 8.0,
     'L0_ffn_b1': 3.042,
     'L0_ffn_b2': 3.496,
     'L0_attn_bo': 8.0}
    for name, (base, spread) in spreads.items():
        noise = np.random.default_rng([zlib.crc32(name.encode()), seed]).standard_normal(out[name].shape)
        drawn = base * np.exp(spread * noise) if base else spread * noise
        out[name] = jnp.asarray(drawn.astype(out[name].dtype))
    for name, factor in factors.items():
        out[name] = (out[name] * factor).astype(out[name].dtype)
    return out
```

```python
from contextlib import ExitStack

import concourse.bass as bass
from concourse import mybir

F32 = mybir.dt.float32
ALU = mybir.AluOpType
ACT = mybir.ActivationFunctionType
AX = mybir.AxisListType

P = 128
NIT = 4
TOK = 1024
EPS = 1e-5
AL, BB, CC, BI, CWT, CB, BDT, B2, DV, ID, MK = 0, 64, 128, 192, 200, 216, 220, 224, 240, 244, 372
NCOL = 404
NR, NG, NZ, ND, NW = 6, 6, 6, 3, 2


class Plan:

    def __init__(self):
        self.queues = {e: [] for e in ("pe", "act", "dve", "pool", "sp")}
        self.count = {}
        self.owner = {}
        self.at = {}
        self.seen = {e: {} for e in self.queues}

    def wait(self, engine, *keys):
        for key in keys:
            sem, value = self.at[key]
            if self.seen[engine].get(sem, 0) < value:
                self.seen[engine][sem] = value
                self.queues[engine].append(("wait", sem, value))

    def op(self, engine, fn, key=None, step=1, sem=None):
        if key is not None:
            sem = sem or key[0]
            assert self.owner.setdefault(sem, engine) == engine
            self.count[sem] = self.count.get(sem, 0) + step
            self.at[key] = (sem, self.count[sem])
        self.queues[engine].append(("op", fn, sem if key is not None else None, step))

    def emit(self, engine, eng, sems):
        for item in self.queues[engine]:
            if item[0] == "wait":
                eng.wait_ge(sems[item[1]], item[2])
            else:
                ins = item[1](eng)
                if item[2] is not None:
                    ins.then_inc(sems[item[2]], item[3])


def build(nc, x, w1a, w2t, wit, wdt, wot, bo, cols, out):
    ctx = ExitStack()
    with ctx:
        def sb(name, shape):
            return ctx.enter_context(nc.sbuf_tensor(name, shape, F32))

        def psb(name, shape):
            return ctx.enter_context(nc.psum_tensor(name, shape, F32))

        COL = sb("COL", [P, NCOL])
        X = sb("X", [P, 2, 8, 256])
        XN = sb("XN", [P, 4, 256])
        XT = sb("XT", [P, 2, TOK])
        WA = sb("WA", [P, NW, 2, 257])
        WB = sb("WB", [P, NW, 2, 256])
        MT = sb("MT", [P, 2, 2, 2, 256])
        HB = sb("HB", [P, 2, 2, 256])
        WI = sb("WI", [P, 2, 1024])
        WD = sb("WD", [32, 512])
        WO = sb("WO", [P, 4, 256])
        BO = sb("BO", [P, 256])
        ONES = sb("ONES", [P, 128])
        RW = sb("RW", [P, 64, 32])
        NAC = sb("NAC", [P, 64])
        BC = sb("BC", [P, 64])
        B2H = sb("B2H", [P, 16])
        BCOL = sb("BCOL", [P, 2])
        DM = sb("DM", [P, 2])
        STT = sb("STT", [P, 64])
        HAL = sb("HAL", [P, 4, 3])
        BNS = sb("BNS", [P, 2, 4, 6])
        MV = sb("MV", [P, 2, 4, 2])
        LV = sb("LV", [P, 2, 5, 4])
        XI = sb("XI", [P, 2, TOK + 3])
        SC = sb("SC", [P, TOK])
        MS = SC[:, 0:514].rearrange("p (i n) -> p i n", i=2)
        DG = SC[:, 520:776].rearrange("p (i n) -> p i n", i=2)
        DW = sb("DW", [P, ND, 2, TOK])
        ZS = sb("ZS", [P, NZ, TOK])
        R = sb("R", [P, NR, 2, TOK])
        G = sb("G", [P, NG, TOK])
        A = psb("A", [P, 2, TOK])
        Y = psb("Y", [P, TOK])
        MB = psb("MB", [P, 2, 512])
        ident = COL[:, ID:ID + 128]

        p = Plan()
        op, wait = p.op, p.wait

        units = []
        pend = []

        def bank(n):
            return MB[:, n % 2, :]

        def unit_open():
            n = len(units)
            units.append(None)
            if n >= 2:
                wait("pe", *units[n - 2])
            return n

        def unit(pe_fn, evac_fn):
            n = unit_open()
            pe_fn(n)
            run_pend()
            pend.append((n, evac_fn))

        def run_pend():
            while pend:
                n, evac = pend.pop(0)
                units[n] = evac(n)

        def load(name, dst, src, queue="sp"):
            op(queue, lambda e: e.dma_start(dst, src), (name,), 16)

        def load_x(it):
            xv = x[TOK * it:TOK * it + TOK, :].rearrange("(i p) d -> p i d", p=P)
            if it >= 2:
                wait("sp", ("store", it - 2, 0), ("store", it - 2, 1))
            for hf in range(2):
                op("sp", lambda e, hf=hf: e.dma_start(X[:, it % 2, 4 * hf:4 * hf + 4, :],
                                                      xv[:, 4 * hf:4 * hf + 4, :]),
                   ("x", it, hf), 16, sem=f"x{hf}")

        nload = [0]

        def load_w(g, c):
            n = 4 * g + c
            assert n == nload[0]
            nload[0] += 1
            if n >= NW:
                wait("sp", ("mm", n - NW))
            s = n % NW
            op("sp", lambda e: e.dma_start(WA[:, s, :, :],
                                           w1a[g].rearrange("(p k) n -> p k n", k=8)[:, 2 * c:2 * c + 2, :]),
               ("wa", n), 16, sem=f"wa{s}")
            op("sp", lambda e: e.dma_start(WB[:, s, :, :],
                                           w2t[g].rearrange("(p k) n -> p k n", k=8)[:, 2 * c:2 * c + 2, :]),
               ("wb", n), 16, sem=f"wb{s}")

        def m_steps(it, hf):
            g = 2 * it + hf
            par = it % 2
            steps = []
            st = {}

            def chunk(c):
                def go():
                    if c == 0:
                        run_pend()
                        st["n"] = unit_open(), unit_open()
                    n = 4 * g + c
                    wait("pe", ("wa", n), ("wb", n))
                    s = n % NW
                    for k in range(2):
                        for i in range(2):
                            last = c == 3 and k == 1
                            op("pe", lambda e, k=k, i=i, last=last: e.matmul(
                                bank(st["n"][i])[:, 0:257], WB[:, s, k, 128 * i:128 * i + 128],
                                WA[:, s, k, :], start=(c == 0 and k == 0), stop=last),
                               ("mm", n) if k == 1 and i == 1 else None)
                    if n + NW < 32:
                        load_w((n + NW) // 4, (n + NW) % 4)
                return go

            def evac():
                wait("act", ("mm", 4 * g + 3))
                if ("mt", g - 1) in p.at:
                    wait("act", ("mt", g - 1), ("bcol", g - 1))
                if ("dt", 4 * it - 1) in p.at:
                    wait("act", ("dt", 4 * it - 1))
                for i in range(2):
                    op("act", lambda e, i=i: e.activation(MS[:, i, :], bank(st["n"][i])[:, 0:257],
                                                          ACT.Copy, scale=0.5), ("ms", g, i))
                    units[st["n"][i]] = (("ms", g, i),)
                wait("pool", ("ms", g, 1), ("b2h",))
                op("pool", lambda e: e.tensor_tensor(BCOL[:, :], MS[:, :, 256], B2H[:, 2 * g:2 * g + 2], ALU.add),
                   ("bcol", g))
                if ("hbm", g - 1) in p.at:
                    wait("pool", ("hbm", g - 1))
                wait("pool", ("bcol", g))
                for i in range(2):
                    op("pool", lambda e, i=i: e.tensor_scalar(DG[:, i, :], ident, BCOL[:, i:i + 1], 0.0,
                                                              ALU.mult, ALU.add), ("dg", g, i))

            def turn():
                def pe(n):
                    wait("pe", ("ms", g, 1))
                    for i in range(2):
                        for j in range(2):
                            op("pe", lambda e, i=i, j=j: e.transpose(
                                bank(n)[:, 256 * j + 128 * i:256 * j + 128 * i + 128],
                                MS[:, i, 128 * j:128 * j + 128], ident), ("mt", g) if i and j else None)

                def ev(n):
                    wait("act", ("mt", g))
                    if it >= 2:
                        wait("act", ("ffn", it - 2, 1, hf, 1))
                    op("act", lambda e: e.activation(MT[:, par, hf, :, :].rearrange("p j n -> p (j n)"),
                                                     bank(n), ACT.Copy), ("mtc", g))
                    return (("mtc", g),)
                unit(pe, ev)

            def bias():
                def pe(n):
                    wait("pe", ("dg", g, 1), ("ones",))
                    for i in range(2):
                        op("pe", lambda e, i=i: e.matmul(bank(n)[:, 128 * i:128 * i + 128], ONES[:, :],
                                                         DG[:, i, :], start=True, stop=True),
                           ("hbm", g) if i else None)

                def ev(n):
                    wait("act", ("hbm", g))
                    if it >= 2:
                        wait("act", ("xb", it - 2, 1, hf))
                    op("act", lambda e: e.activation(HB[:, par, hf, :], bank(n)[:, 0:256], ACT.Copy), ("hb", g))
                    return (("hb", g),)
                unit(pe, ev)

            steps += [chunk(c) for c in range(4)]
            steps += [evac, turn, bias, run_pend]
            return steps

        lncall = [0]
        lnlast = {"xn": None, "conv": None}

        def ln_steps(it, ph, hf):
            v = X[:, it % 2, :, :]
            c = lncall[0]
            lncall[0] += 1
            s = c % 2
            key = (it, ph, hf)
            mv, lv = MV[:, s, :, :], LV[:, s, :, :]

            def stats():
                if ph == 0:
                    wait("dve", ("x", it, hf))
                elif ph == 1:
                    wait("dve", ("ffn", it, 0, hf, 1))
                else:
                    wait("dve", ("op", it, 2 * hf + 1))
                if c >= 2:
                    wait("dve", ("lnt", c - 2), ("lnr", c - 2))
                for i in range(4):
                    op("dve", lambda e, i=i: e.bn_stats(BNS[:, s, i, :], v[:, 4 * hf + i, :]),
                       ("bns", c) if i == 3 else None)

            def aggr():
                wait("dve", ("bns", c))
                for i in range(4):
                    op("dve", lambda e, i=i: e.bn_aggr(mv[:, i, :], BNS[:, s, i, :]), ("bna", c) if i == 3 else None)
                wait("pool", ("bna", c))
                op("pool", lambda e: e.tensor_scalar(lv[:, 0, :], mv[:, :, 1], 1.0, EPS, ALU.mult, ALU.add),
                   ("lnp", c, 0))

            def root():
                wait("act", ("lnp", c, 0))
                op("act", lambda e: e.activation(lv[:, 1, :], lv[:, 0, :], ACT.Ln), ("lnv", c))

            def root2():
                wait("act", ("lnv", c))
                op("act", lambda e: e.activation(lv[:, 1, :], lv[:, 1, :], ACT.Exp, scale=-0.5), ("lnr", c))

            def newton():
                wait("pool", ("lnr", c))
                seq = [
                    lambda e: e.tensor_tensor(lv[:, 2, :], lv[:, 0, :], lv[:, 1, :], ALU.mult),
                    lambda e: e.tensor_tensor(lv[:, 2, :], lv[:, 2, :], lv[:, 1, :], ALU.mult),
                    lambda e: e.tensor_scalar(lv[:, 2, :], lv[:, 2, :], -0.5, 1.5, ALU.mult, ALU.add),
                    lambda e: e.tensor_tensor(lv[:, 3, :], lv[:, 1, :], lv[:, 2, :], ALU.mult),
                    lambda e: e.tensor_tensor(lv[:, 2, :], mv[:, :, 0], lv[:, 3, :], ALU.mult),
                    lambda e: e.tensor_scalar(lv[:, 4, :], lv[:, 2, :], -1.0, 0.0, ALU.mult, ALU.add),
                ]
                for m, fn in enumerate(seq):
                    op("pool", fn, ("lnn", c, m))
                    wait("pool", ("lnn", c, m))

            def norm(i):
                def go():
                    if i == 0:
                        wait("act", ("lnn", c, 5))
                        for k in lnlast["xn"] or ():
                            wait("act", k)
                        if lnlast["conv"]:
                            wait("act", lnlast["conv"])
                    op("act", lambda e: e.activation(XN[:, i, :], v[:, 4 * hf + i, :], ACT.Identity,
                                                     scale=lv[:, 3, i:i + 1], bias=lv[:, 4, i:i + 1]),
                       ("lnt", c) if i == 3 else None)
                    if i == 3:
                        p.at[("norm",) + key] = p.at[("lnt", c)]
                return go

            def turn(j):
                def go():
                    def pe(n):
                        wait("pe", ("norm",) + key)
                        for i in range(4):
                            op("pe", lambda e, i=i: e.transpose(bank(n)[:, 128 * i:128 * i + 128],
                                                                XN[:, i, 128 * j:128 * j + 128], ident),
                               ("xt", c, j) if i == 3 else None)

                    def ev(n):
                        wait("act", ("xt", c, j))
                        for k in xt_free():
                            wait("act", k)
                        op("act", lambda e: e.activation(XT[:, j, 512 * hf:512 * hf + 512], bank(n), ACT.Copy),
                           ("xtc",) + key + (j,))
                        return (("xtc",) + key + (j,),)
                    unit(pe, ev)
                    if j == 1:
                        lnlast["xn"] = [("xt", c, 1)]
                return go

            def skip():
                wait("dve", ("norm",) + key, ("dm",))
                op("dve", lambda e: e.scalar_tensor_tensor(
                    out=v[:, 4 * hf:4 * hf + 4, :], in0=XN[:, :, :], scalar=DM[:, 0:1],
                    in1=v[:, 4 * hf:4 * hf + 4, :], op0=ALU.mult, op1=ALU.add), ("skip", it, hf))
                lnlast["xn"] = [("xt", c, 1), ("skip", it, hf)]
                wait("pool", ("skip", it, hf), ("bo",))
                op("pool", lambda e: e.tensor_tensor(
                    v[:, 4 * hf:4 * hf + 4, :], v[:, 4 * hf:4 * hf + 4, :],
                    BO[:, :].unsqueeze(1).broadcast_to([P, 4, 256]), ALU.add), ("r1", it, hf))

            steps = [stats, aggr, root, root2, newton] + [norm(i) for i in range(4)] + [turn(0), turn(1)]
            if ph == 1:
                steps += [skip]
            return steps

        xt_users = []

        def xt_free():
            return list(xt_users)

        def ffn_steps(it, ph, hf):
            v = X[:, it % 2, :, :]
            par = it % 2
            g = 2 * it + hf

            def pre():
                wait("pool", ("hb", g), ("norm", it, 0 if ph == 0 else 2, hf))
                op("pool", lambda e: e.tensor_tensor(
                    v[:, 4 * hf:4 * hf + 4, :], v[:, 4 * hf:4 * hf + 4, :],
                    HB[:, par, hf, :].unsqueeze(1).broadcast_to([P, 4, 256]), ALU.add), ("xb", it, ph, hf))

            def pair(pr):
                def go():
                    def pe(n):
                        lnp = 0 if ph == 0 else 2
                        wait("pe", ("xtc", it, lnp, hf, 0), ("xtc", it, lnp, hf, 1), ("mtc", g))
                        for i in range(2):
                            for j in range(2):
                                t = 512 * hf + 128 * (2 * pr + i)
                                op("pe", lambda e, i=i, j=j, t=t: e.matmul(
                                    bank(n)[:, 256 * i:256 * i + 256], XT[:, j, t:t + 128],
                                    MT[:, par, hf, j, :], start=(j == 0), stop=(j == 1)),
                                   ("fm", it, ph, hf, pr) if i and j else None)
                        if pr == 1:
                            xt_users.append(("fm", it, ph, hf, pr))

                    def ev(n):
                        wait("dve", ("fm", it, ph, hf, pr), ("xb", it, ph, hf))
                        t = 4 * hf + 2 * pr
                        op("dve", lambda e: e.tensor_tensor(v[:, t:t + 2, :], v[:, t:t + 2, :],
                                                            bank(n).rearrange("p (i d) -> p i d", i=2), ALU.add),
                           ("ffn", it, ph, hf, pr))
                        return (("ffn", it, ph, hf, pr),)
                    unit(pe, ev)
                return go

            def store():
                wait("sp", ("ffn", it, 1, hf, 1))
                ov = out[TOK * it:TOK * it + TOK, :].rearrange("(i p) d -> p i d", p=P)
                op("sp", lambda e: e.dma_start(ov[:, 4 * hf:4 * hf + 4, :], v[:, 4 * hf:4 * hf + 4, :]),
                   ("store", it, hf), 16, sem=f"store{hf}")

            return [pre, pair(0), pair(1)] + ([run_pend, store] if ph == 1 else [run_pend])

        def xi_steps(it, ct):
            k = 4 * it + ct
            d = k % ND
            b = 0 if ct == 0 else 1
            xi = XI[:, b, :]

            def halo():
                last = ("hal", k - 1) if ct >= 2 else ("hal", k - 4) if ct == 0 and it else None
                if ct == 1 and it:
                    last = ("hal", k - 2)
                if last:
                    wait("pool", last)
                if ct == 0 and it:
                    wait("pool", ("dtm", k - 1, 1))
                if it % 2 == 0:
                    op("pool", lambda e: e.memset(xi[:, 0:3], 0.0), ("halo", k))
                else:
                    wait("pool", ("hal", k - 4))
                    op("pool", lambda e: e.tensor_copy(xi[:, 0:3], HAL[:, ct, :]), ("halo", k))

            def proj(hf):
                def go():
                    def pe(n):
                        if hf == 0:
                            wait("pe", ("wi",))
                        wait("pe", ("xtc", it, 1, hf, 0), ("xtc", it, 1, hf, 1))
                        for j in range(2):
                            op("pe", lambda e, j=j: e.matmul(bank(n), WI[:, j, 128 * ct:128 * ct + 128],
                                                             XT[:, j, 512 * hf:512 * hf + 512],
                                                             start=(j == 0), stop=(j == 1)),
                               ("xim", k, hf) if j else None)

                    def ev(n):
                        wait("act", ("xim", k, hf), ("halo", k))
                        op("act", lambda e: e.activation(xi[:, 3 + 512 * hf:515 + 512 * hf], bank(n), ACT.Identity,
                                                         bias=COL[:, BI + ct:BI + ct + 1]), ("xi", k, hf))
                        return (("xi", k, hf),)
                    unit(pe, ev)
                return go

            def conv():
                run_pend()
                wait("pool", ("xi", k, 0), ("xi", k, 1))
                if k >= ND:
                    wait("pool", *[("rep", 4 * (k - ND) + q) for q in range(4)])
                cv = DW[:, d, 1, :]
                tmp = XN[:, :, :].rearrange("p a b -> p (a b)")
                cw = CWT + 4 * ct
                op("pool", lambda e: e.tensor_scalar(cv, xi[:, 3:3 + TOK], COL[:, cw + 3:cw + 4],
                                                     COL[:, CB + ct:CB + ct + 1], ALU.mult, ALU.add), ("cv", k, 0))
                for q in lnlast["xn"] or ():
                    wait("pool", q)
                for t in range(3):
                    op("pool", lambda e, t=t: e.tensor_scalar(tmp, xi[:, t:t + TOK], COL[:, cw + t:cw + t + 1],
                                                              0.0, ALU.mult, ALU.add), ("ct", k, t))
                    wait("pool", ("ct", k, t), ("cv", k, t))
                    op("pool", lambda e: e.tensor_tensor(cv, cv, tmp, ALU.add), ("cv", k, t + 1))
                    wait("pool", ("cv", k, t + 1))
                lnlast["conv"] = ("cv", k, 3)
                op("pool", lambda e: e.tensor_copy(HAL[:, ct, :], xi[:, TOK:TOK + 3]), ("hal", k))

            return [halo, proj(0), proj(1), conv]

        def dt_steps(it, ct):
            k = 4 * it + ct
            d = k % ND

            def mm(hf):
                def go():
                    def pe(n):
                        wait("pe", ("xi", 4 * it, hf), ("wd",))
                        op("pe", lambda e: e.matmul(bank(n), WD[:, 128 * ct:128 * ct + 128],
                                                    XI[0:32, 0, 3 + 512 * hf:515 + 512 * hf], start=True, stop=True),
                           ("dtm", k, hf))

                    def ev(n):
                        wait("dve", ("dtm", k, hf))
                        if k >= ND:
                            wait("dve", *[("rep", 4 * (k - ND) + q) for q in range(4)])
                        op("dve", lambda e: e.tensor_scalar(DW[:, d, 0, 512 * hf:512 * hf + 512], bank(n),
                                                            COL[:, BDT + ct:BDT + ct + 1], 0.0, ALU.add, ALU.max),
                           ("dtr", k, hf))
                        wait("act", ("dtr", k, hf))
                        if k:
                            wait("act", ("dt", k - 1))
                        if hf == 0:
                            wait("act", ("mt", 2 * it + 1), ("bcol", 2 * it + 1), ("hbm", 2 * it + 1))
                        op("act", lambda e: e.activation(SC[:, 512 * hf:512 * hf + 512], bank(n), ACT.Abs,
                                                         bias=COL[:, BDT + ct:BDT + ct + 1]), ("dta", k, hf))
                        return (("dta", k, hf),)
                    unit(pe, ev)
                return go

            def e1():
                run_pend()
                wait("act", ("dta", k, 1))
                op("act", lambda e: e.activation(SC[:, :], SC[:, :], ACT.Exp, scale=-1.0), ("dte", k))

            def e2():
                wait("act", ("dte", k))
                op("act", lambda e: e.activation(SC[:, :], SC[:, :], ACT.Ln, bias=1.0), ("dtl", k))
                wait("pool", ("dtl", k), ("dtr", k, 1))
                op("pool", lambda e: e.tensor_tensor(DW[:, d, 0, :], DW[:, d, 0, :], SC[:, :], ALU.add), ("dt", k))

            return [mm(0), mm(1), e1, e2]

        def silu_step(it, pr):
            cts = (2 * pr, 2 * pr + 1)

            def z(ct, hf):
                k = 4 * it + ct

                def pe(n):
                    for j in range(2):
                        op("pe", lambda e, j=j: e.matmul(bank(n), WI[:, j, 512 + 128 * ct:640 + 128 * ct],
                                                         XT[:, j, 512 * hf:512 * hf + 512],
                                                         start=(j == 0), stop=(j == 1)),
                           ("zm", k, hf) if j else None)
                    if ct == 3:
                        xt_users.append(("zm", k, hf))

                def ev(n):
                    wait("act", ("zm", k, hf))
                    if k >= NZ:
                        wait("act", ("opm", (k - NZ) // 4, 3))
                    op("act", lambda e: e.activation(ZS[:, k % NZ, 512 * hf:512 * hf + 512], bank(n), ACT.Silu,
                                                     bias=COL[:, BI + 4 + ct:BI + 5 + ct]), ("z", k, hf))
                    return (("z", k, hf),)
                return pe, ev

            def start(ct, hf):
                n = unit_open()
                pe, ev = z(ct, hf)
                pe(n)
                return n, ev

            opened = []

            def first():
                run_pend()
                opened.append(start(cts[0], 0))
                opened.append(start(cts[0], 1))

            def batch():
                for n, ev in opened:
                    units[n] = ev(n)
                more = [start(cts[1], 0), start(cts[1], 1)]
                for ct in cts:
                    k = 4 * it + ct
                    wait("act", ("cv", k, 3))
                    op("act", lambda e, k=k: e.activation(DW[:, k % ND, 1, :], DW[:, k % ND, 1, :], ACT.Silu),
                       ("u", k))
                for n, ev in more:
                    units[n] = ev(n)
                for ct in cts:
                    k = 4 * it + ct
                    wait("pool", ("u", k), ("dt", k))
                    op("pool", lambda e, k=k: e.tensor_tensor(DW[:, k % ND, 1, :], DW[:, k % ND, 1, :],
                                                              DW[:, k % ND, 0, :], ALU.mult), ("w", k))
            return [first, batch]

        def rep(k, q):
            ri = 4 * k + q
            s = ri % NR
            wait("sp", ("w", k), ("dt", k))
            if ri >= NR:
                o = ri - NR
                wait("sp", ("scan", o // 4, 3, o % 4))
            for j in range(4):
                op("sp", lambda e, j=j: e.dma_start(R[32 * j:32 * j + 32, s, :, :],
                                                    DW[32 * q:32 * q + 32, k % ND, :, :]), ("rep", ri), 16, sem=f"rep{s}")

        def aslot(k, m, q):
            return (16 * k + 4 * m + q) % 2

        def gslot(k, m, q):
            return (16 * k + 4 * m + q) % NG

        def before(k, m, q, d):
            s = 16 * k + 4 * m + q - d
            return (s // 16, s // 4 % 4, s % 4)

        def exp(k, m, q):
            idx = (k % 4 * 4 + q) * 4 + m
            rs = (4 * k + q) % NR
            wait("act", ("rep", 4 * k + q), ("nac",))
            if 16 * k + 4 * m + q >= 2:
                wait("act", ("scan",) + before(k, m, q, 2))
            op("act", lambda e: e.activation(A[:, aslot(k, m, q), :], R[:, rs, 0, :], ACT.Exp,
                                             scale=NAC[:, idx:idx + 1]), ("exp", k, m, q))

        def scan(k, m, q):
            idx = (k % 4 * 4 + q) * 4 + m
            rs = (4 * k + q) % NR
            odd = k // 4 % 2
            wait("dve", ("rep", 4 * k + q), ("exp", k, m, q))
            s = 16 * k + 4 * m + q
            if s >= NG:
                o = before(k, m, q, NG)
                wait("dve", ("red", o[0], o[1]))
                if o[0] // 4 % 2 == 0:
                    wait("dve", ("save", o[0], o[1], o[2] // 2))
            if odd:
                wait("dve", ("save", k - 4, m, q // 2))
            init = STT[:, idx:idx + 1] if odd else 0.0
            op("dve", lambda e: e.tensor_tensor_scan(G[:, gslot(k, m, q), :], A[:, aslot(k, m, q), :],
                                                     R[:, rs, 1, :], init, ALU.mult, ALU.add), ("scan", k, m, q))

        def save(k, m, h):
            i0 = (k % 4 * 4 + 2 * h) * 4 + m
            g0 = gslot(k, m, 2 * h)
            wait("dve", ("scan", k, m, 2 * h + 1))
            op("dve", lambda e: e.tensor_copy(STT[:, i0:i0 + 5:4], G[:, g0:g0 + 2, TOK - 1]), ("save", k, m, h))

        def reduce(k, m):
            if k == 0 and m == 0:
                wait("pe", ("rw",))
            wait("pe", ("scan", k, m, 3))
            if m == 0 and k:
                wait("pe", ("yz", k - 1))
            for h in range(2):
                for q in range(4):
                    idx = (k % 4 * 4 + q) * 4 + m
                    op("pe", lambda e, h=h, q=q, idx=idx: e.matmul(
                        Y[32 * q:32 * q + 32, 512 * h:512 * h + 512], RW[:, idx, :],
                        G[:, gslot(k, m, q), 512 * h:512 * h + 512], start=(m == 0), stop=(m == 3)),
                       ("red", k, m) if h and q == 3 else None)

        def yz(k):
            wait("dve", ("red", k, 3), ("z", k, 0), ("z", k, 1))
            op("dve", lambda e: e.tensor_tensor(ZS[:, k % NZ, :], ZS[:, k % NZ, :], Y[:, :], ALU.mult), ("yz", k))

        def out_steps(it):
            v = X[:, it % 2, :, :]
            steps = []
            for pr in range(4):
                def go(pr=pr):
                    def pe(n):
                        wait("pe", ("yz", 4 * it + 3), ("wo",))
                        for i in range(2):
                            for ct in range(4):
                                t = 128 * (2 * pr + i)
                                zs = (4 * it + ct) % NZ
                                op("pe", lambda e, i=i, ct=ct, t=t, zs=zs: e.matmul(
                                    bank(n)[:, 256 * i:256 * i + 256], ZS[:, zs, t:t + 128], WO[:, ct, :],
                                    start=(ct == 0), stop=(ct == 3)), ("opm", it, pr) if i and ct == 3 else None)

                    def ev(n):
                        wait("dve", ("opm", it, pr), ("r1", it, pr // 2))
                        op("dve", lambda e: e.tensor_tensor(v[:, 2 * pr:2 * pr + 2, :], v[:, 2 * pr:2 * pr + 2, :],
                                                            bank(n).rearrange("p (i d) -> p i d", i=2), ALU.add),
                           ("op", it, pr))
                        return (("op", it, pr),)
                    unit(pe, ev)
                steps.append(go)
            return steps + [run_pend]

        load_x(0)
        op("act", lambda e: e.dma_start(COL[:, :], cols), ("col",), 16)
        for c in range(NW):
            load_w(0, c)
        op("act", lambda e: e.dma_start(WI[:, :, :], wit.rearrange("(j p) n -> p j n", p=P)), ("wi",), 16)
        op("act", lambda e: e.dma_start(WD[:, :], wdt), ("wd",), 16)
        op("act", lambda e: e.dma_start(BO[:, :], bo.partition_broadcast(P)), ("bo",), 16)
        op("act", lambda e: e.dma_start(WO[:, :, :], wot.rearrange("(j p) n -> p j n", p=P)), ("wo",), 16)
        op("pool", lambda e: e.memset(ONES[:, :], 1.0), ("ones",))
        wait("pool", ("col",))
        op("pool", lambda e: e.tensor_scalar(B2H[:, :], COL[:, B2:B2 + 16], 0.5, 0.0, ALU.mult, ALU.add), ("b2h",))
        op("act", lambda e: e.activation(NAC[:, :], COL[:, AL:AL + 64], ACT.Exp), ("nae",))
        wait("act", ("col",))
        p.queues["act"].insert(len(p.queues["act"]) - 2, p.queues["act"].pop())
        wait("dve", ("nae",))
        op("dve", lambda e: e.tensor_scalar(NAC[:, :], NAC[:, :], -1.0, None, ALU.mult), ("nac",))
        wait("dve", ("col",))
        op("dve", lambda e: e.tensor_tensor(BC[:, :], COL[:, BB:BB + 64], COL[:, CC:CC + 64], ALU.mult), ("bc",))
        wait("dve", ("bc",))
        op("dve", lambda e: e.tensor_tensor(RW[:, :, :], BC[:, :].unsqueeze(2).broadcast_to([P, 64, 32]),
                                            COL[:, MK:MK + 32].unsqueeze(1).broadcast_to([P, 64, 32]), ALU.mult),
           ("rw",))
        n = unit_open()
        wait("pe", ("col",), ("ones",))
        op("pe", lambda e: e.matmul(bank(0)[:, 0:4], ONES[:, :], COL[:, DV:DV + 4], start=True, stop=True), ("dvm",))
        wait("dve", ("dvm",))
        op("dve", lambda e: e.tensor_reduce(DM[:, 1:2], bank(0)[:, 0:4], AX.X, ALU.add), ("dvs",))
        units[n] = (("dvs",),)
        wait("dve", ("dvs",))
        op("dve", lambda e: e.tensor_scalar(DM[:, 0:1], DM[:, 1:2], 1.0 / 512, None, ALU.mult), ("dm",))

        def go(steps):
            for s in steps:
                s()

        def front_a(it):
            s = []
            for hf in range(2):
                s += ln_steps(it, 0, hf)
                s += m_steps(it, hf)
                s += ffn_steps(it, 0, hf)
            return s

        def front_b(it):
            s = []
            for hf in range(2):
                s += ln_steps(it, 1, hf)
            s += [run_pend]
            return s

        def batch(it, pr):
            a, b = 2 * pr, 2 * pr + 1
            s = xi_steps(it, a) + xi_steps(it, b) + dt_steps(it, a) + dt_steps(it, b)
            return s + silu_step(it, pr)

        def back(it):
            s = []
            for hf in range(2):
                s += ln_steps(it, 2, hf) + [run_pend] + ffn_steps(it, 1, hf)
            return s

        go(front_a(0) + front_b(0) + batch(0, 0))
        for q in range(4):
            rep(0, q)
        reps = [(k, q) for k in range(1, 16) for q in range(4)]
        todo = []
        for k in range(16):
            it, ct = divmod(k, 4)
            steps = []
            if ct == 0:
                if it:
                    steps += out_steps(it - 1)
                steps += batch(it, 1)
                if it + 1 < NIT:
                    steps += [lambda it=it: load_x(it + 1)] if it + 1 < 2 else []
            if ct == 1:
                if it:
                    steps += back(it - 1)
                if 2 <= it + 1 < NIT:
                    steps += [lambda it=it: load_x(it + 1)]
                if it + 1 < NIT:
                    steps += front_a(it + 1)
            if ct == 2 and it + 1 < NIT:
                steps += front_b(it + 1) + batch(it + 1, 0)
            done = 0
            for sub in range(16):
                m, q = divmod(sub, 4)
                exp(k, m, q)
                scan(k, m, q)
                if it % 2 == 0 and q % 2 == 0 and sub >= 2:
                    ps = sub - 1
                    save(k, ps // 4, ps % 4 // 2)
                if q == 0 and sub:
                    reduce(k, m - 1)
                if sub == 1 and k:
                    yz(k - 1)
                upto = len(steps) * sub // 15
                while done < upto:
                    steps[done]()
                    done += 1
                if sub in (2, 3) and k + 1 < 16:
                    rep(k + 1, sub - 2)
                if sub in (12, 13) and k + 1 < 16:
                    rep(k + 1, sub - 10)
            if it % 2 == 0:
                save(k, 3, 1)
            reduce(k, 3)
        yz(15)
        go(out_steps(3) + back(3))
        wait("sp", *[("store", it, hf) for it in range(NIT) for hf in range(2)])

        sems = {name: ctx.enter_context(nc.semaphore("s_" + name)) for name in p.count}
        block = ctx.enter_context(nc.Block())

        @block.sync
        def _(e):
            p.emit("sp", e, sems)

        @block.gpsimd
        def _(e):
            p.emit("pool", e, sems)

        @block.scalar
        def _(e):
            e.preload_act_table_set("natural_log_exp_and_others")
            p.emit("act", e, sems)

        @block.vector
        def _(e):
            p.emit("dve", e, sems)

        @block.tensor
        def _(e):
            p.emit("pe", e, sems)


def kernel(**inputs):
    import numpy as np
    import concourse.bacc as bacc
    from concourse.bass_utils import run_bass_kernel_spmd

    v = {k.replace("L0_", ""): np.asarray(a) for k, a in inputs.items()}

    def states(a):
        return a.reshape(4, 4, 32, 4, 4).transpose(4, 2, 0, 1, 3).reshape(128, 64)

    def chans(a, n):
        return a.reshape(n, 128).T

    ident = np.eye(128, dtype=np.float32)
    mask = np.concatenate([np.eye(32, dtype=np.float32)] * 4, axis=0)
    cols = np.concatenate([
        states(v["attn_A_log"]), states(v["attn_Bm"]), states(v["attn_Cm"]), chans(v["attn_bi"], 8),
        v["attn_conv_w"].reshape(4, 128, 4).transpose(1, 0, 2).reshape(128, 16),
        chans(v["attn_conv_b"], 4), chans(v["attn_bdt"], 4), chans(v["ffn_b2"], 16), chans(v["attn_Dv"], 4),
        ident, mask], axis=1)
    arrays = {
        "x": v["attn_x"].reshape(4096, 256),
        "w1a": np.concatenate([v["ffn_W1"], v["ffn_b1"][:, :, None]], axis=2),
        "w2t": v["ffn_W2"].transpose(0, 2, 1),
        "wit": v["attn_Wi"].T,
        "wdt": v["attn_Wdt"].T,
        "wot": v["attn_Wo"].T,
        "bo": v["attn_bo"],
        "cols": cols,
    }
    arrays = {f"in_{k}": np.ascontiguousarray(a) for k, a in arrays.items()}
    nc = bacc.Bacc("TRN2", target_bir_lowering=False, num_devices=1)
    args = [nc.dram_tensor(k, a.shape, mybir.dt.from_np(a.dtype), kind="ExternalInput").ap()
            for k, a in arrays.items()]
    out = nc.dram_tensor("out_0", (4096, 256), F32, kind="ExternalOutput").ap()
    build(nc, *args, out)
    r = run_bass_kernel_spmd(nc, [arrays], core_ids=[0])
    return r.results[0]["out_0"].reshape(2, 2048, 256)
```

```python
from contextlib import ExitStack

import concourse.bass as bass
from concourse import mybir

F32 = mybir.dt.float32
ALU = mybir.AluOpType
ACT = mybir.ActivationFunctionType
AX = mybir.AxisListType

P = 128
NIT = 4
TOK = 1024
EPS = 1e-5
AL, BB, CC, BI, CWT, CB, BDT, B2, DV, ID, MK = 0, 64, 128, 192, 200, 216, 220, 224, 240, 244, 372
NCOL = 404
NR, NG, NZ, ND, NW = 6, 8, 6, 3, 3


STRANDS = ("scan", "mix", "out", "ffn", "m")
PRIO = {
    "pe": ("m", "mix", "ffn", "out", "scan"),
    "act": ("m", "ffn", "mix", "scan", "out"),
    "dve": ("out", "ffn", "mix", "m", "scan"),
    "pool": ("out", "mix", "ffn", "m", "scan"),
    "sp": ("out", "mix", "ffn", "m", "scan"),
}
BANKS = 4
LATER = -1.0
SLACK = 0.35
HOP = 0.07
ISSUE = 0.73
TIMES = {
    "mm": 0.87, "ms": 0.43, "bcol": 0.12, "dg": 0.28, "mt": 0.45, "mtc": 0.57, "hbm": 0.44, "hb": 0.38,
    "bns": 1.34, "bna": 0.4, "lnp": 0.12, "lnv": 0.2, "lnr": 0.2, "lnn": 0.13, "norm": 0.5, "xt": 0.45,
    "xtc": 0.57, "skip": 1.15, "r1": 2.3, "xb": 2.3, "fm": 1.73, "ffn": 0.66, "halo": 0.12, "xim": 1.72,
    "xi": 0.57, "cv": 1.15, "hal": 0.12, "dtm": 0.86, "dtr": 0.66, "dta": 0.57, "dte": 1.04,
    "dtl": 1.04, "dt": 2.3, "zm": 1.72, "z": 0.57, "u": 1.04, "w": 2.3, "exp": 1.04, "scan": 1.2,
    "save": 0.08, "red": 1.9, "yz": 1.2, "opm": 3.45, "op": 0.66, "table": 1.3, "rw": 1.15,
    "wa": 0.06, "wb": 0.06,
}
DMA_TIMES = {"x": 1.45, "wa": 0.37, "wb": 0.37, "store": 1.45, "rep": 0.7}


class Plan:

    def __init__(self):
        self.engines = ("pe", "act", "dve", "pool", "sp")
        self.strand = "scan"
        self.queues = {(e, s): [] for e in self.engines for s in STRANDS}
        self.waiting = {k: [] for k in self.queues}
        self.open = {k: None for k in self.queues}
        self.at = {}
        self.order = {e: [] for e in self.engines}
        self.units = []
        self.taken = []

    def unit(self):
        self.units.append({"free": None, "bank": None})
        self.takes(len(self.units) - 1)
        return len(self.units) - 1

    def takes(self, n):
        self.taken.append(n)

    def wait(self, engine, *keys):
        for key in keys:
            assert key in self.at, key
        k = (engine, self.strand)
        item = self.open[k]
        if item is None:
            self.waiting[k] += keys
        else:
            item["parts"].append(("wait", keys))
            item["needs"] += keys

    def op(self, engine, fn, key=None, step=1, sem=None, cut=None, hold=False):
        k = (engine, self.strand)
        item = self.open[k]
        if item is None:
            needs = self.waiting[k]
            self.waiting[k] = []
            item = {"needs": list(needs), "parts": [("wait", tuple(needs))], "t": 0.0, "keys": [], "hold": False,
                    "strand": self.strand, "takes": []}
            if engine == "pe":
                item["takes"], self.taken = self.taken, []
            self.queues[k].append(item)
        item["parts"].append(("op", fn, key, step))
        if cut:
            item["t"] = TIMES[cut]
        if key is not None:
            item["t"] = (DMA_TIMES if engine == "sp" else TIMES).get(key[0], 0.15)
            assert key not in self.at
            self.at[key] = (sem or key[0], step, item)
            item["keys"].append(key)
        item["hold"] = hold
        self.open[k] = item if key is None and not cut else None

    def merge(self):
        pos = {k: 0 for k in self.queues}
        free = {e: 0.0 for e in self.engines}
        held = {e: None for e in self.engines}
        done = {}
        dma = 0.0
        banks = [()] * BANKS

        def ready(key, item):
            if key in done:
                return done[key]
            if key in item["keys"] or key[0] in ("mm", "zm"):
                return LATER
            maker = self.at[key][2]
            if maker["takes"]:
                return None
            times = [ready(need, item) for need in maker["needs"] if need not in maker["keys"]]
            return None if None in times or LATER not in times else LATER

        def releases(item):
            at = 0.0
            for n in item["takes"]:
                for key in self.units[n]["free"]:
                    for need in self.at[key][2]["needs"]:
                        if need in self.at[key][2]["keys"]:
                            continue
                        t = ready(need, item)
                        if t is None:
                            return None
                        if t != LATER:
                            at = max(at, t)
            return at - item["t"] - 0.5

        left = sum(len(q) for q in self.queues.values())
        while left:
            best = None
            for e in self.engines:
                cands = []
                for pr, s in enumerate(PRIO[e]):
                    if held[e] not in (None, s) or e == "pe" and held["act"] not in (None, s):
                        continue
                    q = self.queues[e, s]
                    if pos[e, s] >= len(q):
                        continue
                    item = q[pos[e, s]]
                    start = free[e]
                    for key in item["needs"]:
                        if key in item["keys"]:
                            continue
                        d = done.get(key)
                        if d is None:
                            break
                        start = max(start, d + HOP)
                    else:
                        if item["takes"]:
                            open_at = sorted(max([done[x] for x in b] or [0.0]) for b in banks
                                             if all(x in done for x in b))
                            could = releases(item)
                            if len(open_at) < len(item["takes"]) or could is None:
                                continue
                            start = max(start, open_at[len(item["takes"]) - 1] + HOP, could)
                        cands.append((start, pr, s, item))
                if not cands:
                    continue
                first = min(c[0] for c in cands)
                c = min((c for c in cands if c[0] <= first + SLACK), key=lambda c: c[1])
                if best is None or c[0] < best[0]:
                    best = (c[0], e, c[2], c[3])
            assert best is not None, "the strands wait for each other"
            start, e, s, item = best
            for n in item["takes"]:
                b = min((b for b in range(BANKS) if all(x in done for x in banks[b])),
                        key=lambda b: max([done[x] for x in banks[b]] or [0.0]))
                item["parts"].insert(0, ("wait", banks[b]))
                banks[b] = self.units[n]["free"]
                self.units[n]["bank"] = b
            free[e] = end = start + item["t"]
            if item["keys"] and item["keys"][0][0] in ("wa", "wb"):
                dma = max(dma, start + ISSUE) + DMA_TIMES["wa"]
                end = dma + 1.6
            if e == "sp":
                free[e] = start + ISSUE
                dma = max(dma, start + ISSUE) + item["t"]
                end = dma + 1.6
            for key in item["keys"]:
                done[key] = end
            held[e] = s if item["hold"] else None
            self.order[e].append(item)
            pos[e, s] += 1
            left -= 1
        self.end = max(free.values())

    def count(self):
        self.values, self.owner, self.total = {}, {}, {}
        for e in self.engines:
            for item in self.order[e]:
                for part in item["parts"]:
                    if part[0] == "op" and part[2] is not None:
                        sem = self.at[part[2]][0]
                        assert self.owner.setdefault(sem, e) == e
                        self.total[sem] = self.total.get(sem, 0) + part[3]
                        self.values[part[2]] = self.total[sem]

    def emit(self, engine, eng, sems):
        seen = {}
        for item in self.order[engine]:
            for part in item["parts"]:
                if part[0] == "wait":
                    for key in part[1]:
                        sem, value = self.at[key][0], self.values[key]
                        if seen.get(sem, 0) < value:
                            seen[sem] = value
                            eng.wait_ge(sems[sem], value)
                elif part[1] is not None:
                    ins = part[1](eng)
                    if part[2] is not None:
                        ins.then_inc(sems[self.at[part[2]][0]], part[3])


def build(nc, x, w1a, w2t, wit, wdt, wot, bo, cols, out):
    ctx = ExitStack()
    with ctx:
        def sb(name, shape):
            return ctx.enter_context(nc.sbuf_tensor(name, shape, F32))

        def psb(name, shape):
            return ctx.enter_context(nc.psum_tensor(name, shape, F32))

        COL = sb("COL", [P, NCOL])
        X = sb("X", [P, 2, 8, 256])
        XN = sb("XN", [P, 4, 256])
        XT = sb("XT", [P, 2, TOK])
        WA = sb("WA", [P, NW, 257])
        WB = sb("WB", [P, NW, 256])
        MT = sb("MT", [P, 2, 2, 2, 256])
        HB = sb("HB", [P, 2, 2, 256])
        WI = sb("WI", [P, 2, 1024])
        WD = sb("WD", [32, 512])
        WO = sb("WO", [P, 4, 256])
        BO = sb("BO", [P, 256])
        ONES = sb("ONES", [P, 1])
        RW = sb("RW", [P, 2, 16, 32])
        B2H = sb("B2H", [P, 16])
        BCOL = sb("BCOL", [P, 2])
        DM = sb("DM", [P, 2])
        STT = sb("STT", [P, 64])
        HAL = sb("HAL", [P, 4, 3])
        BNS = sb("BNS", [P, 2, 4, 6])
        MV = sb("MV", [P, 2, 4, 2])
        LV = sb("LV", [P, 2, 5, 4])
        XI = sb("XI", [P, 2, TOK + 3])
        SC = sb("SC", [P, TOK])
        MS = SC[:, 0:514].rearrange("p (i n) -> p i n", i=2)
        DG = SC[:, 520:776].rearrange("p (i n) -> p i n", i=2)
        DW = sb("DW", [P, ND, 2, TOK])
        ZS = sb("ZS", [P, NZ, TOK])
        R = sb("R", [P, NR, 2, TOK])
        G = sb("G", [P, NG, TOK])
        Y = psb("Y", [P, 2, TOK])
        MB = psb("MB", [P, BANKS, 512])
        NAC, BC = COL[:, AL:AL + 64], COL[:, BB:BB + 64]
        ident = COL[:, ID:ID + 128]

        p = Plan()
        op, wait = p.op, p.wait

        pend = []

        def bank(n):
            return MB[:, p.units[n]["bank"], :]

        unit_open = p.unit

        def unit(pe_fn, evac_fn):
            n = unit_open()
            pe_fn(n)
            run_pend()
            pend.append((n, evac_fn, p.strand))

        def run_pend():
            here = p.strand
            while pend:
                n, evac, p.strand = pend.pop(0)
                p.units[n]["free"] = evac(n)
            p.strand = here

        def within(strand, steps):
            def make(fn):
                def go():
                    here, p.strand = p.strand, strand
                    fn()
                    p.strand = here
                return go
            return [make(fn) for fn in steps]

        def load(name, dst, src, queue="sp"):
            op(queue, lambda e: e.dma_start(dst, src), (name,), 16)

        def load_x(it):
            xv = x[TOK * it:TOK * it + TOK, :].rearrange("(i p) d -> p i d", p=P)
            if it >= 2:
                wait("sp", ("store", it - 2, 0), ("store", it - 2, 1))
            for hf in range(2):
                op("sp", lambda e, hf=hf: e.dma_start(X[:, it % 2, 4 * hf:4 * hf + 4, :],
                                                      xv[:, 4 * hf:4 * hf + 4, :]),
                   ("x", it, hf), 16, sem=f"x{hf}")

        nload = [0]

        def load_w(g, c):
            n = 8 * g + c
            assert n == nload[0]
            nload[0] += 1
            if n >= NW:
                wait("act", ("mm", n - NW))
            s = n % NW
            op("act", lambda e: e.dma_start(WA[:, s, :], w1a[g].rearrange("(p k) n -> p k n", k=8)[:, c, :]),
               ("wa", n), 16, sem=f"wa{s}")
            op("act", lambda e: e.dma_start(WB[:, s, :], w2t[g].rearrange("(p k) n -> p k n", k=8)[:, c, :]),
               ("wb", n), 16, sem=f"wb{s}")

        def m_steps(it, hf):
            g = 2 * it + hf
            par = it % 2
            steps = []
            st = {}

            def chunk(c):
                def go():
                    if c == 0:
                        run_pend()
                        st["n"] = unit_open(), unit_open()
                    n = 8 * g + c
                    wait("pe", ("wa", n), ("wb", n))
                    s = n % NW
                    for i in range(2):
                        op("pe", lambda e, i=i: e.matmul(
                            bank(st["n"][i])[:, 0:257], WB[:, s, 128 * i:128 * i + 128],
                            WA[:, s, :], start=(c == 0), stop=(c == 7)),
                           ("mm", n) if i == 1 else None)
                    if n + NW < 64:
                        load_w((n + NW) // 8, (n + NW) % 8)
                return go

            def evac():
                wait("act", ("mm", 8 * g + 7))
                if ("mt", g - 1) in p.at:
                    wait("act", ("mt", g - 1), ("bcol", g - 1))
                if ("dt", 4 * it - 1) in p.at:
                    wait("act", ("dt", 4 * it - 1))
                for i in range(2):
                    op("act", lambda e, i=i: e.activation(MS[:, i, :], bank(st["n"][i])[:, 0:257],
                                                          ACT.Copy, scale=0.5), ("ms", g, i))
                    p.units[st["n"][i]]["free"] = (("ms", g, i),)
                wait("pool", ("ms", g, 1), ("b2h",))
                op("pool", lambda e: e.tensor_tensor(BCOL[:, :], MS[:, :, 256], B2H[:, 2 * g:2 * g + 2], ALU.add),
                   ("bcol", g))
                if ("hbm", g - 1) in p.at:
                    wait("pool", ("hbm", g - 1))
                wait("pool", ("bcol", g))
                for i in range(2):
                    op("pool", lambda e, i=i: e.tensor_scalar(DG[:, i, :], ident, BCOL[:, i:i + 1], 0.0,
                                                              ALU.mult, ALU.add), ("dg", g, i))

            def turn():
                def pe(n):
                    wait("pe", ("ms", g, 1))
                    for i in range(2):
                        for j in range(2):
                            op("pe", lambda e, i=i, j=j: e.transpose(
                                bank(n)[:, 256 * j + 128 * i:256 * j + 128 * i + 128],
                                MS[:, i, 128 * j:128 * j + 128], ident), ("mt", g) if i and j else None)

                def ev(n):
                    wait("act", ("mt", g))
                    if it >= 2:
                        wait("act", ("ffn", it - 2, 1, hf, 1))
                    op("act", lambda e: e.activation(MT[:, par, hf, :, :].rearrange("p j n -> p (j n)"),
                                                     bank(n), ACT.Copy), ("mtc", g))
                    return (("mtc", g),)
                unit(pe, ev)

            def bias():
                def pe(n):
                    wait("pe", ("dg", g, 1), ("ones",))
                    for i in range(2):
                        op("pe", lambda e, i=i: e.matmul(bank(n)[:, 128 * i:128 * i + 128], ONES[:, 0:1].broadcast_to([P, P]),
                                                         DG[:, i, :], start=True, stop=True),
                           ("hbm", g) if i else None)

                def ev(n):
                    wait("act", ("hbm", g))
                    if it >= 2:
                        wait("act", ("xb", it - 2, 1, hf))
                    op("act", lambda e: e.activation(HB[:, par, hf, :], bank(n)[:, 0:256], ACT.Copy), ("hb", g))
                    return (("hb", g),)
                unit(pe, ev)

            steps += [chunk(c) for c in range(8)]
            steps += [evac, turn, bias, run_pend]
            return steps

        lncall = [0]
        norms = []
        lnlast = {"xn": None, "conv": None}

        def ln_steps(it, ph, hf):
            v = X[:, it % 2, :, :]
            c = lncall[0]
            lncall[0] += 1
            norms.append(("norm", it, ph, hf))
            s = c % 2
            key = (it, ph, hf)
            mv, lv = MV[:, s, :, :], LV[:, s, :, :]

            def stats():
                if ph == 0:
                    wait("dve", ("x", it, hf))
                elif ph == 1:
                    wait("dve", ("ffn", it, 0, hf, 1))
                else:
                    wait("dve", ("op", it, 2 * hf + 1))
                if c >= 2:
                    wait("dve", norms[c - 2], ("lnr", c - 2))
                for i in range(4):
                    op("dve", lambda e, i=i: e.bn_stats(BNS[:, s, i, :], v[:, 4 * hf + i, :]),
                       ("bns", c) if i == 3 else None)

            def aggr():
                wait("dve", ("bns", c))
                for i in range(4):
                    op("dve", lambda e, i=i: e.bn_aggr(mv[:, i, :], BNS[:, s, i, :]), ("bna", c) if i == 3 else None)
                wait("pool", ("bna", c))
                op("pool", lambda e: e.tensor_scalar(lv[:, 0, :], mv[:, :, 1], 1.0, EPS, ALU.mult, ALU.add),
                   ("lnp", c, 0))

            def root():
                wait("act", ("lnp", c, 0))
                op("act", lambda e: e.activation(lv[:, 1, :], lv[:, 0, :], ACT.Ln), ("lnv", c))

            def root2():
                wait("act", ("lnv", c))
                op("act", lambda e: e.activation(lv[:, 1, :], lv[:, 1, :], ACT.Exp, scale=-0.5), ("lnr", c))

            def newton():
                wait("pool", ("lnr", c))
                seq = [
                    lambda e: e.tensor_tensor(lv[:, 2, :], lv[:, 0, :], lv[:, 1, :], ALU.mult),
                    lambda e: e.tensor_tensor(lv[:, 2, :], lv[:, 2, :], lv[:, 1, :], ALU.mult),
                    lambda e: e.tensor_scalar(lv[:, 2, :], lv[:, 2, :], -0.5, 1.5, ALU.mult, ALU.add),
                    lambda e: e.tensor_tensor(lv[:, 3, :], lv[:, 1, :], lv[:, 2, :], ALU.mult),
                    lambda e: e.tensor_tensor(lv[:, 2, :], mv[:, :, 0], lv[:, 3, :], ALU.mult),
                    lambda e: e.tensor_scalar(lv[:, 4, :], lv[:, 2, :], -1.0, 0.0, ALU.mult, ALU.add),
                ]
                for m, fn in enumerate(seq):
                    op("pool", fn, ("lnn", c, m))
                    wait("pool", ("lnn", c, m))

            def norm(i):
                def go():
                    if i == 0:
                        wait("act", ("lnn", c, 5), *(lnlast["xn"] or ()))
                    op("act", lambda e: e.activation(XN[:, i, :], v[:, 4 * hf + i, :], ACT.Identity,
                                                     scale=lv[:, 3, i:i + 1], bias=lv[:, 4, i:i + 1]),
                       ("norm",) + key if i == 3 else None, cut="norm" if i < 3 else None)
                return go

            def turn(j):
                def go():
                    def pe(n):
                        wait("pe", ("norm",) + key)
                        for i in range(4):
                            op("pe", lambda e, i=i: e.transpose(bank(n)[:, 128 * i:128 * i + 128],
                                                                XN[:, i, 128 * j:128 * j + 128], ident),
                               ("xt", c, j) if i == 3 else None)

                    def ev(n):
                        wait("act", ("xt", c, j))
                        wait("act", *xt_users[hf])
                        if j == 1:
                            xt_users[hf] = []
                        op("act", lambda e: e.activation(XT[:, j, 512 * hf:512 * hf + 512], bank(n), ACT.Copy),
                           ("xtc",) + key + (j,))
                        return (("xtc",) + key + (j,),)
                    unit(pe, ev)
                    if j == 1:
                        lnlast["xn"] = [("xt", c, 1)]
                return go

            def skip():
                wait("dve", ("norm",) + key, ("dm",))
                op("dve", lambda e: e.scalar_tensor_tensor(
                    out=v[:, 4 * hf:4 * hf + 4, :], in0=XN[:, :, :], scalar=DM[:, 0:1],
                    in1=v[:, 4 * hf:4 * hf + 4, :], op0=ALU.mult, op1=ALU.add), ("skip", it, hf))
                lnlast["xn"] = [("xt", c, 1), ("skip", it, hf)]
                wait("pool", ("skip", it, hf), ("bo",))
                op("pool", lambda e: e.tensor_tensor(
                    v[:, 4 * hf:4 * hf + 4, :], v[:, 4 * hf:4 * hf + 4, :],
                    BO[:, :].unsqueeze(1).broadcast_to([P, 4, 256]), ALU.add), ("r1", it, hf))

            steps = [norm(i) for i in range(4)] + [turn(0), turn(1)]
            if ph == 1:
                steps += [skip]
            return [stats, aggr, root, root2, newton], steps

        xt_users = {0: [], 1: []}

        def ffn_steps(it, ph, hf):
            v = X[:, it % 2, :, :]
            par = it % 2
            g = 2 * it + hf

            def pre():
                wait("pool", ("hb", g), ("norm", it, 0 if ph == 0 else 2, hf))
                op("pool", lambda e: e.tensor_tensor(
                    v[:, 4 * hf:4 * hf + 4, :], v[:, 4 * hf:4 * hf + 4, :],
                    HB[:, par, hf, :].unsqueeze(1).broadcast_to([P, 4, 256]), ALU.add), ("xb", it, ph, hf))

            def pair(pr):
                def go():
                    def pe(n):
                        lnp = 0 if ph == 0 else 2
                        wait("pe", ("xtc", it, lnp, hf, 0), ("xtc", it, lnp, hf, 1), ("mtc", g))
                        for i in range(2):
                            for j in range(2):
                                t = 512 * hf + 128 * (2 * pr + i)
                                op("pe", lambda e, i=i, j=j, t=t: e.matmul(
                                    bank(n)[:, 256 * i:256 * i + 256], XT[:, j, t:t + 128],
                                    MT[:, par, hf, j, :], start=(j == 0), stop=(j == 1)),
                                   ("fm", it, ph, hf, pr) if i and j else None)
                        if pr == 1:
                            xt_users[hf] = [("fm", it, ph, hf, pr)]

                    def ev(n):
                        wait("dve", ("fm", it, ph, hf, pr), ("xb", it, ph, hf))
                        t = 4 * hf + 2 * pr
                        op("dve", lambda e: e.tensor_tensor(v[:, t:t + 2, :], v[:, t:t + 2, :],
                                                            bank(n).rearrange("p (i d) -> p i d", i=2), ALU.add),
                           ("ffn", it, ph, hf, pr))
                        return (("ffn", it, ph, hf, pr),)
                    unit(pe, ev)
                return go

            def store():
                wait("sp", ("ffn", it, 1, hf, 1))
                ov = out[TOK * it:TOK * it + TOK, :].rearrange("(i p) d -> p i d", p=P)
                op("sp", lambda e: e.dma_start(ov[:, 4 * hf:4 * hf + 4, :], v[:, 4 * hf:4 * hf + 4, :]),
                   ("store", it, hf), 16, sem=f"store{hf}")

            return [pre, pair(0), pair(1)] + ([run_pend, store] if ph == 1 else [run_pend])

        def xi_steps(it, ct):
            k = 4 * it + ct
            d = k % ND
            b = 0 if ct == 0 else 1
            xi = XI[:, b, :]

            def halo():
                last = ("hal", k - 1) if ct >= 2 else ("hal", k - 4) if ct == 0 and it else None
                if ct == 1 and it:
                    last = ("hal", k - 2)
                if last:
                    wait("pool", last)
                if ct == 0 and it:
                    wait("pool", ("dtm", k - 1, 1))
                if it % 2 == 0:
                    op("pool", lambda e: e.memset(xi[:, 0:3], 0.0), ("halo", k))
                else:
                    wait("pool", ("hal", k - 4))
                    op("pool", lambda e: e.tensor_copy(xi[:, 0:3], HAL[:, ct, :]), ("halo", k))

            def proj(hf):
                def go():
                    def pe(n):
                        if hf == 0:
                            wait("pe", ("wi",))
                        wait("pe", ("xtc", it, 1, hf, 0), ("xtc", it, 1, hf, 1))
                        for j in range(2):
                            op("pe", lambda e, j=j: e.matmul(bank(n), WI[:, j, 128 * ct:128 * ct + 128],
                                                             XT[:, j, 512 * hf:512 * hf + 512],
                                                             start=(j == 0), stop=(j == 1)),
                               ("xim", k, hf) if j else None)

                    def ev(n):
                        wait("act", ("xim", k, hf), ("halo", k))
                        op("act", lambda e: e.activation(xi[:, 3 + 512 * hf:515 + 512 * hf], bank(n), ACT.Identity,
                                                         bias=COL[:, BI + ct:BI + ct + 1]), ("xi", k, hf))
                        return (("xi", k, hf),)
                    unit(pe, ev)
                return go

            def conv():
                run_pend()
                wait("dve", ("xi", k, 0), ("xi", k, 1))
                if k >= ND:
                    wait("dve", *[("rep", 4 * (k - ND) + q) for q in range(4)])
                cv = DW[:, d, 1, :]
                cw = CWT + 4 * ct
                op("dve", lambda e: e.tensor_scalar(cv, xi[:, 3:3 + TOK], COL[:, cw + 3:cw + 4],
                                                    COL[:, CB + ct:CB + ct + 1], ALU.mult, ALU.add), ("cv", k, 0))
                for t in range(3):
                    wait("dve", ("cv", k, t))
                    op("dve", lambda e, t=t: e.scalar_tensor_tensor(
                        out=cv, in0=xi[:, t:t + TOK], scalar=COL[:, cw + t:cw + t + 1], in1=cv,
                        op0=ALU.mult, op1=ALU.add), ("cv", k, t + 1))
                wait("pool", ("cv", k, 3))
                op("pool", lambda e: e.tensor_copy(HAL[:, ct, :], xi[:, TOK:TOK + 3]), ("hal", k))

            return [halo, proj(0), proj(1), conv]

        def dt_steps(it, ct):
            k = 4 * it + ct
            d = k % ND

            def mm(hf):
                def go():
                    def pe(n):
                        wait("pe", ("xi", 4 * it, hf), ("wd",))
                        op("pe", lambda e: e.matmul(bank(n), WD[:, 128 * ct:128 * ct + 128],
                                                    XI[0:32, 0, 3 + 512 * hf:515 + 512 * hf], start=True, stop=True),
                           ("dtm", k, hf))

                    def ev(n):
                        wait("dve", ("dtm", k, hf))
                        if k >= ND:
                            wait("dve", *[("rep", 4 * (k - ND) + q) for q in range(4)])
                        op("dve", lambda e: e.tensor_scalar(DW[:, d, 0, 512 * hf:512 * hf + 512], bank(n),
                                                            COL[:, BDT + ct:BDT + ct + 1], 0.0, ALU.add, ALU.max),
                           ("dtr", k, hf))
                        wait("act", ("dtr", k, hf))
                        if k:
                            wait("act", ("dt", k - 1))
                        if hf == 0:
                            wait("act", ("mt", 2 * it + 1), ("bcol", 2 * it + 1), ("hbm", 2 * it + 1))
                        op("act", lambda e: e.activation(SC[:, 512 * hf:512 * hf + 512], bank(n), ACT.Abs,
                                                         bias=COL[:, BDT + ct:BDT + ct + 1]), ("dta", k, hf))
                        return (("dta", k, hf),)
                    unit(pe, ev)
                return go

            def e1():
                run_pend()
                wait("act", ("dta", k, 1))
                op("act", lambda e: e.activation(SC[:, :], SC[:, :], ACT.Exp, scale=-1.0), ("dte", k))

            def e2():
                wait("act", ("dte", k))
                op("act", lambda e: e.activation(SC[:, :], SC[:, :], ACT.Ln, bias=1.0), ("dtl", k))
                wait("pool", ("dtl", k), ("dtr", k, 1))
                op("pool", lambda e: e.tensor_tensor(DW[:, d, 0, :], DW[:, d, 0, :], SC[:, :], ALU.add), ("dt", k))

            return [mm(0), mm(1), e1, e2]

        def silu_step(it, pr):
            cts = (2 * pr, 2 * pr + 1)

            def z(ct, hf):
                k = 4 * it + ct

                def pe(n):
                    for j in range(2):
                        op("pe", lambda e, j=j: e.matmul(bank(n), WI[:, j, 512 + 128 * ct:640 + 128 * ct],
                                                         XT[:, j, 512 * hf:512 * hf + 512],
                                                         start=(j == 0), stop=(j == 1)),
                           ("zm", k, hf) if j else None)
                    if ct == 3:
                        xt_users[hf] = [("zm", k, hf)]

                def ev(n):
                    wait("act", ("zm", k, hf))
                    wait("act", ("cv", k, 3), *([("zm", k, 1)] if ct == cts[0] else []))
                    if k >= NZ:
                        wait("act", ("opm", (k - NZ) // 4, 3))
                    op("act", lambda e: e.activation(ZS[:, k % NZ, 512 * hf:512 * hf + 512], bank(n), ACT.Silu,
                                                     bias=COL[:, BI + 4 + ct:BI + 5 + ct]), ("z", k, hf), hold=True)
                    return (("z", k, hf),)
                return pe, ev

            def start(ct, hf):
                n = unit_open()
                pe, ev = z(ct, hf)
                pe(n)
                return n, ev

            opened = []

            def first():
                run_pend()
                opened.append(start(cts[0], 0))
                opened.append(start(cts[0], 1))

            def batch():
                for n, ev in opened:
                    p.units[n]["free"] = ev(n)
                more = [start(cts[1], 0), start(cts[1], 1)]
                for ct in cts:
                    k = 4 * it + ct
                    wait("act", ("cv", k, 3))
                    op("act", lambda e, k=k: e.activation(DW[:, k % ND, 1, :], DW[:, k % ND, 1, :], ACT.Silu),
                       ("u", k), hold=True)
                for n, ev in more:
                    p.units[n]["free"] = ev(n)
                op("act", lambda e: e.preload_act_table_set("natural_log_exp_and_others"), cut="table")
                for ct in cts:
                    k = 4 * it + ct
                    wait("pool", ("u", k), ("dt", k))
                    op("pool", lambda e, k=k: e.tensor_tensor(DW[:, k % ND, 1, :], DW[:, k % ND, 1, :],
                                                              DW[:, k % ND, 0, :], ALU.mult), ("w", k))
            return [first, batch]

        def rep(k, q):
            ri = 4 * k + q
            s = ri % NR
            wait("sp", ("w", k), ("dt", k))
            if ri >= NR:
                o = ri - NR
                wait("sp", ("scan", o // 4, 3, o % 4))
            for j in range(4):
                op("sp", lambda e, j=j: e.dma_start(R[32 * j:32 * j + 32, s, :, :],
                                                    DW[32 * q:32 * q + 32, k % ND, :, :]),
                   ("rep", ri) if j == 3 else ("rep", ri, j), 16, sem=f"rep{s}")

        def gslot(k, m, q):
            return (16 * k + 4 * m + q) % NG

        def before(k, m, q, d):
            s = 16 * k + 4 * m + q - d
            return (s // 16, s // 4 % 4, s % 4)

        def exp(k, m, q):
            idx = (k % 4 * 4 + q) * 4 + m
            rs = (4 * k + q) % NR
            wait("act", ("rep", 4 * k + q), ("nac",))
            if 16 * k + 4 * m + q >= NG:
                o = before(k, m, q, NG)
                wait("act", ("red", o[0], o[1]))
                if o[0] // 4 % 2 == 0:
                    wait("act", ("save", o[0], o[1], o[2] // 2))
            op("act", lambda e: e.activation(G[:, gslot(k, m, q), :], R[:, rs, 0, :], ACT.Exp,
                                             scale=NAC[:, idx:idx + 1]), ("exp", k, m, q))

        def scan(k, m, q):
            idx = (k % 4 * 4 + q) * 4 + m
            rs = (4 * k + q) % NR
            odd = k // 4 % 2
            wait("dve", ("rep", 4 * k + q), ("exp", k, m, q))
            if odd:
                wait("dve", ("save", k - 4, m, q // 2))
            init = STT[:, idx:idx + 1] if odd else 0.0
            op("dve", lambda e: e.tensor_tensor_scan(G[:, gslot(k, m, q), :], G[:, gslot(k, m, q), :],
                                                     R[:, rs, 1, :], init, ALU.mult, ALU.add), ("scan", k, m, q))

        def save(k, m, h):
            i0 = (k % 4 * 4 + 2 * h) * 4 + m
            g0 = gslot(k, m, 2 * h)
            wait("dve", ("scan", k, m, 2 * h + 1))
            op("dve", lambda e: e.tensor_copy(STT[:, i0:i0 + 5:4], G[:, g0:g0 + 2, TOK - 1]), ("save", k, m, h))

        def rw(k):
            wait("pool", ("bc",), ("red", k - 2, 3)) if k >= 2 else wait("pool", ("bc",))
            c0 = 16 * (k % 4)
            op("pool", lambda e: e.tensor_tensor(
                RW[:, k % 2, :, :], BC[:, c0:c0 + 16].unsqueeze(2).broadcast_to([P, 16, 32]),
                COL[:, MK:MK + 32].unsqueeze(1).broadcast_to([P, 16, 32]), ALU.mult), ("rw", k))

        def reduce(k, m):
            wait("pe", ("rw", k))
            wait("pe", ("scan", k, m, 3))
            if m == 0 and k >= 2:
                wait("pe", ("yz", k - 2))
            for h in range(2):
                for q in range(4):
                    idx = 4 * q + m
                    op("pe", lambda e, h=h, q=q, idx=idx: e.matmul(
                        Y[32 * q:32 * q + 32, k % 2, 512 * h:512 * h + 512], RW[:, k % 2, idx, :],
                        G[:, gslot(k, m, q), 512 * h:512 * h + 512], start=(m == 0), stop=(m == 3)),
                       ("red", k, m) if h and q == 3 else None)

        def yz(k):
            wait("dve", ("red", k, 3), ("z", k, 0), ("z", k, 1))
            op("dve", lambda e: e.tensor_tensor(ZS[:, k % NZ, :], ZS[:, k % NZ, :], Y[:, k % 2, :], ALU.mult), ("yz", k))

        def out_steps(it):
            v = X[:, it % 2, :, :]
            steps = []
            for pr in range(4):
                def go(pr=pr):
                    def pe(n):
                        wait("pe", ("yz", 4 * it + 3), ("wo",))
                        for i in range(2):
                            for ct in range(4):
                                t = 128 * (2 * pr + i)
                                zs = (4 * it + ct) % NZ
                                op("pe", lambda e, i=i, ct=ct, t=t, zs=zs: e.matmul(
                                    bank(n)[:, 256 * i:256 * i + 256], ZS[:, zs, t:t + 128], WO[:, ct, :],
                                    start=(ct == 0), stop=(ct == 3)), ("opm", it, pr) if i and ct == 3 else None)

                    def ev(n):
                        wait("dve", ("opm", it, pr), ("r1", it, pr // 2))
                        op("dve", lambda e: e.tensor_tensor(v[:, 2 * pr:2 * pr + 2, :], v[:, 2 * pr:2 * pr + 2, :],
                                                            bank(n).rearrange("p (i d) -> p i d", i=2), ALU.add),
                           ("op", it, pr))
                        return (("op", it, pr),)
                    unit(pe, ev)
                steps.append(go)
            return within("out", steps + [run_pend])

        load_x(0)
        op("act", lambda e: e.dma_start(COL[:, :], cols), ("col",), 16)
        for c in range(NW):
            load_w(0, c)
        op("act", lambda e: e.dma_start(WI[:, :, :], wit.rearrange("(j p) n -> p j n", p=P)), ("wi",), 16)
        op("act", lambda e: e.dma_start(WD[:, :], wdt), ("wd",), 16)
        op("act", lambda e: e.dma_start(BO[:, :], bo.partition_broadcast(P)), ("bo",), 16)
        op("act", lambda e: e.dma_start(WO[:, :, :], wot.rearrange("(j p) n -> p j n", p=P)), ("wo",), 16)
        op("pool", lambda e: e.memset(ONES[:, :], 1.0), ("ones",))
        wait("pool", ("col",))
        op("pool", lambda e: e.tensor_scalar(B2H[:, :], COL[:, B2:B2 + 16], 0.5, 0.0, ALU.mult, ALU.add), ("b2h",))
        wait("act", ("col",))
        op("act", lambda e: e.activation(NAC, NAC, ACT.Exp), ("nae",))
        wait("dve", ("nae",))
        op("dve", lambda e: e.tensor_scalar(NAC, NAC, -1.0, None, ALU.mult), ("nac",))
        wait("dve", ("col",))
        op("dve", lambda e: e.tensor_tensor(BC, BC, COL[:, CC:CC + 64], ALU.mult), ("bc",))
        n = unit_open()
        wait("pe", ("col",), ("ones",))
        op("pe", lambda e: e.matmul(bank(n)[:, 0:4], ONES[:, 0:1].broadcast_to([P, P]), COL[:, DV:DV + 4], start=True, stop=True), ("dvm",))
        wait("dve", ("dvm",))
        op("dve", lambda e: e.tensor_reduce(DM[:, 1:2], bank(n)[:, 0:4], AX.X, ALU.add), ("dvs",))
        p.units[n]["free"] = (("dvs",),)
        wait("dve", ("dvs",))
        op("dve", lambda e: e.tensor_scalar(DM[:, 0:1], DM[:, 1:2], 1.0 / 512, None, ALU.mult), ("dm",))

        def go(steps):
            for s in steps:
                s()

        def front(it):
            m = [within("m", m_steps(it, hf)) for hf in range(2)]
            s1, n1 = zip(*[ln_steps(it, 0, hf) for hf in range(2)])
            s2, n2 = zip(*[ln_steps(it, 1, hf) for hf in range(2)])
            f = [ffn_steps(it, 0, hf) for hf in range(2)]
            ffn = lambda steps: within("ffn", steps)
            return (ffn(s1[0] + s1[1] + n1[0]) + m[0] + ffn(f[0] + s2[0] + n1[1]) + m[1]
                    + ffn(f[1] + n2[0] + s2[1] + n2[1] + [run_pend]))

        def batch(it, pr):
            a, b = 2 * pr, 2 * pr + 1
            s = xi_steps(it, a) + xi_steps(it, b) + dt_steps(it, a) + dt_steps(it, b)
            return within("mix", s + silu_step(it, pr))

        def back(it):
            s3, n3 = zip(*[ln_steps(it, 2, hf) for hf in range(2)])
            f = [ffn_steps(it, 1, hf) for hf in range(2)]
            return within("ffn", s3[0] + s3[1] + n3[0] + [run_pend] + f[0] + n3[1] + [run_pend] + f[1])

        go(front(0) + batch(0, 0))
        for q in range(4):
            rep(0, q)
        rw(0)
        reps = [(k, q) for k in range(1, 16) for q in range(4)]
        todo = []
        for k in range(16):
            it, ct = divmod(k, 4)
            steps = []
            if ct == 0:
                if it:
                    steps += out_steps(it - 1)
                steps += batch(it, 1)
                if it + 1 < NIT:
                    steps += [lambda it=it: load_x(it + 1)] if it + 1 < 2 else []
            if ct == 1:
                if it:
                    steps += back(it - 1)
                if 2 <= it + 1 < NIT:
                    steps += [lambda it=it: load_x(it + 1)]
                if it + 1 < NIT:
                    steps += front(it + 1)
            if ct == 2 and it + 1 < NIT:
                steps += batch(it + 1, 0)
            done = 0
            for sub in range(16):
                m, q = divmod(sub, 4)
                exp(k, m, q)
                scan(k, m, q)
                if it % 2 == 0 and q % 2 == 0 and sub >= 2:
                    ps = sub - 1
                    save(k, ps // 4, ps % 4 // 2)
                if q == 0 and sub:
                    reduce(k, m - 1)
                if sub == 1 and k:
                    yz(k - 1)
                upto = len(steps) * sub // 15
                while done < upto:
                    steps[done]()
                    done += 1
                if sub == 4 and k + 1 < 16:
                    rw(k + 1)
                if sub in (2, 3) and k + 1 < 16:
                    rep(k + 1, sub - 2)
                if sub in (12, 13) and k + 1 < 16:
                    rep(k + 1, sub - 10)
            if it % 2 == 0:
                save(k, 3, 1)
            reduce(k, 3)
        yz(15)
        go(out_steps(3) + back(3))
        wait("sp", *[("store", it, hf) for it in range(NIT) for hf in range(2)])

        op("sp", None, cut="table")

        p.merge()
        p.count()
        sems = {name: ctx.enter_context(nc.semaphore("s_" + name)) for name in p.total}
        block = ctx.enter_context(nc.Block())

        @block.sync
        def _(e):
            p.emit("sp", e, sems)

        @block.gpsimd
        def _(e):
            p.emit("pool", e, sems)

        @block.scalar
        def _(e):
            e.preload_act_table_set("natural_log_exp_and_others")
            p.emit("act", e, sems)

        @block.vector
        def _(e):
            p.emit("dve", e, sems)

        @block.tensor
        def _(e):
            p.emit("pe", e, sems)


def kernel(**inputs):
    import numpy as np
    import concourse.bacc as bacc
    from concourse.bass_utils import run_bass_kernel_spmd

    v = {k.replace("L0_", ""): np.asarray(a) for k, a in inputs.items()}

    def states(a):
        return a.reshape(4, 4, 32, 4, 4).transpose(4, 2, 0, 1, 3).reshape(128, 64)

    def chans(a, n):
        return a.reshape(n, 128).T

    ident = np.eye(128, dtype=np.float32)
    mask = np.concatenate([np.eye(32, dtype=np.float32)] * 4, axis=0)
    cols = np.concatenate([
        states(v["attn_A_log"]), states(v["attn_Bm"]), states(v["attn_Cm"]), chans(v["attn_bi"], 8),
        v["attn_conv_w"].reshape(4, 128, 4).transpose(1, 0, 2).reshape(128, 16),
        chans(v["attn_conv_b"], 4), chans(v["attn_bdt"], 4), chans(v["ffn_b2"], 16), chans(v["attn_Dv"], 4),
        ident, mask], axis=1)
    arrays = {
        "x": v["attn_x"].reshape(4096, 256),
        "w1a": np.concatenate([v["ffn_W1"], v["ffn_b1"][:, :, None]], axis=2),
        "w2t": v["ffn_W2"].transpose(0, 2, 1),
        "wit": v["attn_Wi"].T,
        "wdt": v["attn_Wdt"].T,
        "wot": v["attn_Wo"].T,
        "bo": v["attn_bo"],
        "cols": cols,
    }
    arrays = {f"in_{k}": np.ascontiguousarray(a) for k, a in arrays.items()}
    nc = bacc.Bacc("TRN2", target_bir_lowering=False, num_devices=1)
    args = [nc.dram_tensor(k, a.shape, mybir.dt.from_np(a.dtype), kind="ExternalInput").ap()
            for k, a in arrays.items()]
    out = nc.dram_tensor("out_0", (4096, 256), F32, kind="ExternalOutput").ap()
    build(nc, *args, out)
    r = run_bass_kernel_spmd(nc, [arrays], core_ids=[0])
    return r.results[0]["out_0"].reshape(2, 2048, 256)
```
